# Optimizing a Trainium2 kernel written in Bass

```python
import numpy as np
import jax
import jax.numpy as jnp

def _softmax(x, axis=-1):
    return jax.nn.softmax(x, axis=axis)

def _gelu(x):
    return jax.nn.gelu(x, approximate=True)

def _silu(x):
    return jax.nn.silu(x)

def _sigmoid(x):
    return jax.nn.sigmoid(x)

def _layernorm(x, axis=-1, eps=1e-05):
    m = jnp.mean(x, axis=axis, keepdims=True)
    v = jnp.var(x, axis=axis, keepdims=True)
    return (x - m) / jnp.sqrt(v + eps)

def _scatter_add(tgt, idx, src, axis=0):
    return tgt.at[idx].add(src)

def _segment_sum(src, seg, n):
    return jax.ops.segment_sum(src, seg, n)
kernel_name = 'mk_dlrm_tower_d1_rec_r8_845043'

def setup_inputs(seed: int=0):
    np.random.seed(seed)
    _w = jnp.asarray

    def _rec_inputs():
        import jax
        import jax.numpy as jnp
        _tk = jax.random.key(seed)
        dense_ctx = jax.random.normal(jax.random.fold_in(_tk, 190), (512, 16), jnp.float32)
        ids = jnp.stack([jax.random.randint(jax.random.fold_in(_tk, 200 + f), (512,), 0, v, jnp.int32) for f, v in enumerate([1000, 1000, 1250, 1000, 1000, 125000, 125000, 1000, 1000, 125000, 12500, 125000, 1250, 1000, 12500, 1000, 1250, 125000, 12500, 125000, 1000, 1000, 1000, 1000, 1000, 1000, 1000, 125000, 1000, 12500, 1250, 1000, 125000, 1000, 1250, 125000, 12500, 1250, 1250])], axis=1)
        tbl_0 = 0.05 * jax.random.normal(jax.random.fold_in(_tk, 500 + 0), (1000, 16), jnp.float32)
        tbl_1 = 0.05 * jax.random.normal(jax.random.fold_in(_tk, 500 + 1), (1000, 16), jnp.float32)
        tbl_2 = 0.05 * jax.random.normal(jax.random.fold_in(_tk, 500 + 2), (1250, 16), jnp.float32)
        tbl_3 = 0.05 * jax.random.normal(jax.random.fold_in(_tk, 500 + 3), (1000, 16), jnp.float32)
        tbl_4 = 0.05 * jax.random.normal(jax.random.fold_in(_tk, 500 + 4), (1000, 16), jnp.float32)
        tbl_5 = 0.05 * jax.random.normal(jax.random.fold_in(_tk, 500 + 5), (125000, 16), jnp.float32)
        tbl_6 = 0.05 * jax.random.normal(jax.random.fold_in(_tk, 500 + 6), (125000, 16), jnp.float32)
        tbl_7 = 0.05 * jax.random.normal(jax.random.fold_in(_tk, 500 + 7), (1000, 16), jnp.float32)
        tbl_8 = 0.05 * jax.random.normal(jax.random.fold_in(_tk, 500 + 8), (1000, 16), jnp.float32)
        tbl_9 = 0.05 * jax.random.normal(jax.random.fold_in(_tk, 500 + 9), (125000, 16), jnp.float32)
        tbl_10 = 0.05 * jax.random.normal(jax.random.fold_in(_tk, 500 + 10), (12500, 16), jnp.float32)
        tbl_11 = 0.05 * jax.random.normal(jax.random.fold_in(_tk, 500 + 11), (125000, 16), jnp.float32)
        tbl_12 = 0.05 * jax.random.normal(jax.random.fold_in(_tk, 500 + 12), (1250, 16), jnp.float32)
        tbl_13 = 0.05 * jax.random.normal(jax.random.fold_in(_tk, 500 + 13), (1000, 16), jnp.float32)
        tbl_14 = 0.05 * jax.random.normal(jax.random.fold_in(_tk, 500 + 14), (12500, 16), jnp.float32)
        tbl_15 = 0.05 * jax.random.normal(jax.random.fold_in(_tk, 500 + 15), (1000, 16), jnp.float32)
        tbl_16 = 0.05 * jax.random.normal(jax.random.fold_in(_tk, 500 + 16), (1250, 16), jnp.float32)
        tbl_17 = 0.05 * jax.random.normal(jax.random.fold_in(_tk, 500 + 17), (125000, 16), jnp.float32)
        tbl_18 = 0.05 * jax.random.normal(jax.random.fold_in(_tk, 500 + 18), (12500, 16), jnp.float32)
        tbl_19 = 0.05 * jax.random.normal(jax.random.fold_in(_tk, 500 + 19), (125000, 16), jnp.float32)
        tbl_20 = 0.05 * jax.random.normal(jax.random.fold_in(_tk, 500 + 20), (1000, 16), jnp.float32)
        tbl_21 = 0.05 * jax.random.normal(jax.random.fold_in(_tk, 500 + 21), (1000, 16), jnp.float32)
        tbl_22 = 0.05 * jax.random.normal(jax.random.fold_in(_tk, 500 + 22), (1000, 16), jnp.float32)
        tbl_23 = 0.05 * jax.random.normal(jax.random.fold_in(_tk, 500 + 23), (1000, 16), jnp.float32)
        tbl_24 = 0.05 * jax.random.normal(jax.random.fold_in(_tk, 500 + 24), (1000, 16), jnp.float32)
        tbl_25 = 0.05 * jax.random.normal(jax.random.fold_in(_tk, 500 + 25), (1000, 16), jnp.float32)
        tbl_26 = 0.05 * jax.random.normal(jax.random.fold_in(_tk, 500 + 26), (1000, 16), jnp.float32)
        tbl_27 = 0.05 * jax.random.normal(jax.random.fold_in(_tk, 500 + 27), (125000, 16), jnp.float32)
        tbl_28 = 0.05 * jax.random.normal(jax.random.fold_in(_tk, 500 + 28), (1000, 16), jnp.float32)
        tbl_29 = 0.05 * jax.random.normal(jax.random.fold_in(_tk, 500 + 29), (12500, 16), jnp.float32)
        tbl_30 = 0.05 * jax.random.normal(jax.random.fold_in(_tk, 500 + 30), (1250, 16), jnp.float32)
        tbl_31 = 0.05 * jax.random.normal(jax.random.fold_in(_tk, 500 + 31), (1000, 16), jnp.float32)
        tbl_32 = 0.05 * jax.random.normal(jax.random.fold_in(_tk, 500 + 32), (125000, 16), jnp.float32)
        tbl_33 = 0.05 * jax.random.normal(jax.random.fold_in(_tk, 500 + 33), (1000, 16), jnp.float32)
        tbl_34 = 0.05 * jax.random.normal(jax.random.fold_in(_tk, 500 + 34), (1250, 16), jnp.float32)
        tbl_35 = 0.05 * jax.random.normal(jax.random.fold_in(_tk, 500 + 35), (125000, 16), jnp.float32)
        tbl_36 = 0.05 * jax.random.normal(jax.random.fold_in(_tk, 500 + 36), (12500, 16), jnp.float32)
        tbl_37 = 0.05 * jax.random.normal(jax.random.fold_in(_tk, 500 + 37), (1250, 16), jnp.float32)
        tbl_38 = 0.05 * jax.random.normal(jax.random.fold_in(_tk, 500 + 38), (1250, 16), jnp.float32)
        _rk = jax.random.fold_in(_tk, 7)
        W_top1 = 0.0693375 * jax.random.normal(jax.random.fold_in(_tk, 801), (208, 512), jnp.float32)
        W_top2 = 0.0441942 * jax.random.normal(jax.random.fold_in(_tk, 802), (512, 256), jnp.float32)
        W_top3 = 0.0625 * jax.random.normal(jax.random.fold_in(_tk, 803), (256, 1), jnp.float32)
        b_top1 = jnp.zeros((512,), jnp.float32)
        b_top2 = jnp.zeros((256,), jnp.float32)
        return (dense_ctx, ids, tbl_0, tbl_1, tbl_2, tbl_3, tbl_4, tbl_5, tbl_6, tbl_7, tbl_8, tbl_9, tbl_10, tbl_11, tbl_12, tbl_13, tbl_14, tbl_15, tbl_16, tbl_17, tbl_18, tbl_19, tbl_20, tbl_21, tbl_22, tbl_23, tbl_24, tbl_25, tbl_26, tbl_27, tbl_28, tbl_29, tbl_30, tbl_31, tbl_32, tbl_33, tbl_34, tbl_35, tbl_36, tbl_37, tbl_38, W_top1, b_top1, W_top2, b_top2, W_top3)
    dense_ctx, ids, tbl_0, tbl_1, tbl_2, tbl_3, tbl_4, tbl_5, tbl_6, tbl_7, tbl_8, tbl_9, tbl_10, tbl_11, tbl_12, tbl_13, tbl_14, tbl_15, tbl_16, tbl_17, tbl_18, tbl_19, tbl_20, tbl_21, tbl_22, tbl_23, tbl_24, tbl_25, tbl_26, tbl_27, tbl_28, tbl_29, tbl_30, tbl_31, tbl_32, tbl_33, tbl_34, tbl_35, tbl_36, tbl_37, tbl_38, W_top1, b_top1, W_top2, b_top2, W_top3 = _rec_inputs()

    def _L0_rec_setup():
        import jax, jax.numpy as jnp
        import numpy as np
        key = jax.random.key(seed)
        k1, k2, k3 = jax.random.split(key, 3)
        B, F0, D = (1024, 39, 16)
        L = 128
        hash_x = jax.random.normal(k1, (B, F0, D), dtype=jnp.float32)
        W0 = jax.random.normal(k2, (F0 * F0, L), dtype=jnp.float32) * 0.05
        W1 = jax.random.normal(k3, (F0 * (L // 2), L), dtype=jnp.float32) * 0.05
        return {'hash_x': hash_x, 'W0': W0, 'W1': W1}
    _L0_rec_all = _L0_rec_setup()
    _L0_rec_in = {k: v for k, v in _L0_rec_all.items() if k in ('W0', 'W1')}
    del _L0_rec_all
    return {'dense_ctx': dense_ctx, 'ids': ids, 'tbl_0': tbl_0, 'tbl_1': tbl_1, 'tbl_2': tbl_2, 'tbl_3': tbl_3, 'tbl_4': tbl_4, 'tbl_5': tbl_5, 'tbl_6': tbl_6, 'tbl_7': tbl_7, 'tbl_8': tbl_8, 'tbl_9': tbl_9, 'tbl_10': tbl_10, 'tbl_11': tbl_11, 'tbl_12': tbl_12, 'tbl_13': tbl_13, 'tbl_14': tbl_14, 'tbl_15': tbl_15, 'tbl_16': tbl_16, 'tbl_17': tbl_17, 'tbl_18': tbl_18, 'tbl_19': tbl_19, 'tbl_20': tbl_20, 'tbl_21': tbl_21, 'tbl_22': tbl_22, 'tbl_23': tbl_23, 'tbl_24': tbl_24, 'tbl_25': tbl_25, 'tbl_26': tbl_26, 'tbl_27': tbl_27, 'tbl_28': tbl_28, 'tbl_29': tbl_29, 'tbl_30': tbl_30, 'tbl_31': tbl_31, 'tbl_32': tbl_32, 'tbl_33': tbl_33, 'tbl_34': tbl_34, 'tbl_35': tbl_35, 'tbl_36': tbl_36, 'tbl_37': tbl_37, 'tbl_38': tbl_38, 'W_top1': W_top1, 'b_top1': b_top1, 'W_top2': W_top2, 'b_top2': b_top2, 'W_top3': W_top3, 'L0_rec_W0': _L0_rec_in['W0'], 'L0_rec_W1': _L0_rec_in['W1']}

def reference(dense_ctx, ids, tbl_0, tbl_1, tbl_2, tbl_3, tbl_4, tbl_5, tbl_6, tbl_7, tbl_8, tbl_9, tbl_10, tbl_11, tbl_12, tbl_13, tbl_14, tbl_15, tbl_16, tbl_17, tbl_18, tbl_19, tbl_20, tbl_21, tbl_22, tbl_23, tbl_24, tbl_25, tbl_26, tbl_27, tbl_28, tbl_29, tbl_30, tbl_31, tbl_32, tbl_33, tbl_34, tbl_35, tbl_36, tbl_37, tbl_38, W_top1, b_top1, W_top2, b_top2, W_top3, L0_rec_W0, L0_rec_W1):
    import jax
    import jax.numpy as jnp

    def _L0_rec_ref(hash_x, W0, W1):
        import jax, jax.numpy as jnp
        import numpy as np
        x0 = hash_x
        B, F0, D = x0.shape
        L = W0.shape[1]
        z0 = jnp.einsum('bid,bjd->bdij', x0, x0).reshape(B, D, F0 * F0)
        cur0 = jax.nn.relu(jnp.einsum('bdk,kl->bld', z0, W0))
        next_h, direct0 = jnp.split(cur0, 2, axis=1)
        Fk = next_h.shape[1]
        z1 = jnp.einsum('bid,bjd->bdij', x0, next_h).reshape(B, D, F0 * Fk)
        cur1 = jax.nn.relu(jnp.einsum('bdk,kl->bld', z1, W1))
        result = jnp.concatenate([direct0, cur1], axis=1)
        return jnp.sum(result, axis=-1)
    e = jnp.stack([tbl_0[ids[:, 0]], tbl_1[ids[:, 1]], tbl_2[ids[:, 2]], tbl_3[ids[:, 3]], tbl_4[ids[:, 4]], tbl_5[ids[:, 5]], tbl_6[ids[:, 6]], tbl_7[ids[:, 7]], tbl_8[ids[:, 8]], tbl_9[ids[:, 9]], tbl_10[ids[:, 10]], tbl_11[ids[:, 11]], tbl_12[ids[:, 12]], tbl_13[ids[:, 13]], tbl_14[ids[:, 14]], tbl_15[ids[:, 15]], tbl_16[ids[:, 16]], tbl_17[ids[:, 17]], tbl_18[ids[:, 18]], tbl_19[ids[:, 19]], tbl_20[ids[:, 20]], tbl_21[ids[:, 21]], tbl_22[ids[:, 22]], tbl_23[ids[:, 23]], tbl_24[ids[:, 24]], tbl_25[ids[:, 25]], tbl_26[ids[:, 26]], tbl_27[ids[:, 27]], tbl_28[ids[:, 28]], tbl_29[ids[:, 29]], tbl_30[ids[:, 30]], tbl_31[ids[:, 31]], tbl_32[ids[:, 32]], tbl_33[ids[:, 33]], tbl_34[ids[:, 34]], tbl_35[ids[:, 35]], tbl_36[ids[:, 36]], tbl_37[ids[:, 37]], tbl_38[ids[:, 38]]], axis=1)
    z = _L0_rec_ref(e, L0_rec_W0, L0_rec_W1)
    z = z.reshape(z.shape[0], -1)
    h = jnp.concatenate([z, dense_ctx], axis=1)
    h = jnp.maximum(h @ W_top1 + b_top1, 0.0)
    h = jnp.maximum(h @ W_top2 + b_top2, 0.0)
    y = h @ W_top3
    return y

_drawn_inputs = setup_inputs


def setup_inputs(seed=0):
    import zlib

    import numpy as np

    out = dict(_drawn_inputs(seed))
    spreads = {'b_top1': (0.0, 0.8), 'b_top2': (0.0, 0.453)}
    factors = {'tbl_0': 8.0,
     'tbl_1': 8.0,
     'tbl_2': 8.0,
     'tbl_3': 8.0,
     'tbl_4': 8.0,
     'tbl_5': 8.0,
     'tbl_6': 8.0,
     'tbl_7': 8.0,
     'tbl_8': 8.0,
     'tbl_9': 8.0,
     'tbl_10': 8.0,
     'tbl_11': 8.0,
     'tbl_12': 8.0,
     'tbl_13': 8.0,
     'tbl_14': 8.0,
     'tbl_15': 8.0,
     'tbl_16': 8.0,
     'tbl_17': 8.0,
     'tbl_18': 8.0,
     'tbl_19': 8.0,
     'tbl_20': 8.0,
     'tbl_21': 8.0,
     'tbl_22': 8.0,
     'tbl_23': 8.0,
     'tbl_24': 8.0,
     'tbl_25': 8.0,
     'tbl_26': 8.0,
     'tbl_27': 8.0,
     'tbl_28': 8.0,
     'tbl_29': 8.0,
     'tbl_30': 8.0,
     'tbl_31': 8.0,
     'tbl_32': 8.0,
     'tbl_33': 8.0,
     'tbl_34': 8.0,
     'tbl_35': 8.0,
     'tbl_36': 8.0,
     'tbl_37': 8.0,
     'tbl_38': 8.0,
     'L0_rec_W1': 8.0}
    for name, (base, spread) in spreads.items():
        noise = np.random.default_rng([zlib.crc32(name.encode()), seed]).standard_normal(out[name].shape)
        drawn = base * np.exp(spread * noise) if base else spread * noise
        out[name] = jnp.asarray(drawn.astype(out[name].dtype))
    for name, factor in factors.items():
        out[name] = (out[name] * factor).astype(out[name].dtype)
    return out
```

```python
from contextlib import ExitStack

import numpy as np
import concourse.bass as bass
from concourse import mybir

ALU = mybir.AluOpType
ACT = mybir.ActivationFunctionType
F32 = mybir.dt.float32
BF16 = mybir.dt.bfloat16
I32 = mybir.dt.int32
AX_X = mybir.AxisListType.X

P = 128
F = 39
D = 16
B = 512
NF1 = 64
L = 128
PARTS = 3
XR = PARTS * F
BT = B // P
DC = 4
NC = DC * P
Q = D // DC
CH = BT * Q
SHIFTS = F // 2 + 1
T0 = -(-SHIFTS // 3)
T1 = -(-F // 2)
K0 = [F * min(3, SHIFTS - 3 * g) for g in range(T0)]
K1 = [NF1 * min(2, F - 2 * t) for t in range(T1)]
RING = 4
AHEAD = RING - 1
PER = T0 + T1
ITEMS = 1 + PER
H1, H2 = 512, 256
M1, M2 = H1 // P, H2 // P
DENSE = 16
T_AT = 10
CUR1_SUM_AT, DIRECT_SUM_AT = 3, T0 + 3
UNROLL = Q
LOOPS = (CH - 2) // UNROLL
assert ITEMS % RING == 0 and (1 + T0) % RING == 0


def spread_matrix():
    cols = [[p % F for p in range(XR)]]
    cols += [[(p % F + 3 * g + p // F) % F for p in range(K0[g])] for g in range(T0)]
    cols += [[2 * t + p // NF1 for p in range(K1[t])] for t in range(T1)]
    m = np.zeros((XR, 1 + T0 + T1, P), np.float32)
    for c, picks in enumerate(cols):
        for p, i in enumerate(picks):
            m[i::F, c, p] = 1.0
    return m


def tower(nc, ids, dense_t, tables, spread_c, ident_c, w0a, w0b, w1, wt1, b1, wt2, b2, wt3, out):
    with ExitStack() as ctx:
        def sb(name, shape, dt=F32):
            return ctx.enter_context(nc.sbuf_tensor(name, shape, dt))

        def bank(name):
            return ctx.enter_context(nc.psum_tensor(name, [P, NC], F32))

        def sem(name):
            return ctx.enter_context(nc.semaphore(name))

        ids_sb = sb("ids_sb", [P, BT * F], I32)
        spread = sb("spread", [XR, 1 + T0 + T1, P], BF16)
        ident = sb("ident", [P, P], BF16)
        w0_ij = sb("w0_ij", [XR, T0, L])
        w0_ji = sb("w0_ji", [XR, T0, L])
        w0_sum = sb("w0_sum", [XR, T0, L])
        w1_sb = sb("w1_sb", [P, T1, L])
        wt1_a = sb("wt1_a", [P, H1])
        wt1_b = sb("wt1_b", [P, H1])
        wt2_sb = sb("wt2_sb", [P, M1, H2])
        wt3_sb = sb("wt3_sb", [P, M2])
        b1_sb = sb("b1_sb", [P, M1])
        b2_sb = sb("b2_sb", [P, M2])
        e = sb("e", [P, BT, F * D])
        rest = sb("rest", [P, D, F])
        parts = sb("parts", [P, BT * D, PARTS, F], BF16)
        xp = sb("xp", [XR, Q, NC], BF16)
        x3 = sb("x3", [XR, NC])
        hh = sb("hh", [P, 2, NC])
        prod = sb("prod", [P, RING, NC])
        direct = sb("direct", [P, NC])
        cur1 = sb("cur1", [P, NC])
        direct_q = sb("direct_q", [P, CH, P])
        cur1_q = sb("cur1_q", [P, CH, P])
        zin_a = sb("zin_a", [P, B])
        zin_b = sb("zin_b", [P, B])
        h1_sb = sb("h1_sb", [P, M1, B])
        h2_sb = sb("h2_sb", [P, M2, B])
        y_sb = sb("y_sb", [1, B])

        ring = [bank(f"ring{r}") for r in range(RING)]
        acc0 = bank("acc0")
        acc1 = bank("acc1")
        xt_ps = bank("xt_ps")
        y_ps = bank("y_ps")

        ids_in = sem("ids_in")
        spread_in = sem("spread_in")
        ident_in = sem("ident_in")
        w0_in = sem("w0_in")
        w1_in = sem("w1_in")
        mlp_in = sem("mlp_in")
        gathered = [sem(f"gathered{t}") for t in range(BT)]
        split_step = sem("split_step")
        zeroed = sem("zeroed")
        w0_ready = sem("w0_ready")
        transposed = sem("transposed")
        xp_ready = sem("xp_ready")
        x3_spread = sem("x3_spread")
        x3_ready = sem("x3_ready")
        spread_done = sem("spread_done")
        prod_ready = sem("prod_ready")
        contracted = sem("contracted")
        h_ready = sem("h_ready")
        cur1_ready = sem("cur1_ready")
        direct_summed = sem("direct_summed")
        cur1_summed = sem("cur1_summed")
        zin_step = sem("zin_step")
        h1_mm = sem("h1_mm")
        h1_ready = sem("h1_ready")
        h2_mm = sem("h2_mm")
        h2_ready = sem("h2_ready")
        y_mm = sem("y_mm")
        y_ready = sem("y_ready")
        stored = sem("stored")

        block = ctx.enter_context(nc.Block())

        FIRST, LAST = (0, -1), (0, CH - 1)

        def chunk(c, more=0):
            return c[0] * UNROLL + (c[1] + more)

        def at(c, where):
            return isinstance(c[0], int) and c == where

        def made(c, k):
            if at(c, FIRST):
                return k
            return c[0] * (UNROLL * PER) + (T0 + c[1] * PER + k - (T0 if at(c, LAST) else 0))

        def products(c):
            return range(T0) if at(c, FIRST) else range(T0, PER) if at(c, LAST) else range(PER)

        def items(c):
            return ([] if at(c, LAST) else [0]) + [k + 1 for k in products(c)]

        def run_steps(engine, step):
            step((0, 0), (0, 1))
            with engine.Fori(0, LOOPS) as i:
                for r in range(1, 1 + UNROLL):
                    step((i, r), (i, r + 1))
            for c in range(1 + LOOPS * UNROLL, CH):
                step((0, c), (0, c + 1) if c + 1 < CH else None)

        def known_after(c, n):
            return not isinstance(c[0], int) or c[1] + n < CH

        @block.sync
        def _(sp):
            sp.dma_start(ids_sb[:, :], ids).then_inc(ids_in, 16)
            sp.dma_start(ident[:, :], ident_c).then_inc(ident_in, 16)
            sp.dma_start(spread[:, :, :], spread_c).then_inc(spread_in, 16)
            sp.dma_start(w0_ij[:, :, :], w0a).then_inc(w0_in, 16)
            sp.dma_start(w0_ji[:, :, :], w0b).then_inc(w0_in, 16)
            whole = F * NF1 // P
            sp.dma_start(w1_sb[:, 0:whole, :],
                         w1[0:whole * P, :].rearrange("(t p) l -> p t l", p=P)).then_inc(w1_in, 16)
            sp.dma_start(w1_sb[0:K1[-1], whole, :], w1[whole * P:, :]).then_inc(w1_in, 16)
            sp.wait_ge(zeroed, 2)
            sp.dma_start(wt1_a[0:DENSE, :], wt1[NF1 + L:, :]).then_inc(mlp_in, 16)
            sp.dma_start(wt1_a[NF1:P, :], wt1[0:NF1, :]).then_inc(mlp_in, 16)
            sp.dma_start(wt1_b[:, :], wt1[NF1:NF1 + L, :]).then_inc(mlp_in, 16)
            sp.dma_start(zin_a[0:DENSE, :], dense_t).then_inc(mlp_in, 16)
            sp.dma_start(wt2_sb[:, :, :], wt2.rearrange("(m p) n -> p m n", p=P)).then_inc(mlp_in, 16)
            sp.dma_start(wt3_sb[:, :], wt3).then_inc(mlp_in, 16)
            sp.dma_start(b1_sb[:, :], b1).then_inc(mlp_in, 16)
            sp.dma_start(b2_sb[:, :], b2).then_inc(mlp_in, 16)
            sp.wait_ge(y_ready, 1)
            sp.dma_start(out, y_sb[:, :]).then_inc(stored, 16)
            sp.wait_ge(stored, 16)

        MLP_IN = 8 * 16

        @block.gpsimd
        def _(pool):
            def gather(t):
                for f in range(F):
                    pool.indirect_dma_start(
                        out=e[:, t, f * D:(f + 1) * D], out_offset=None, in_=tables[f],
                        in_offset=bass.IndirectOffsetOnAxis(
                            ap=ids_sb[:, t * F + f:t * F + f + 1], axis=0),
                    ).then_inc(gathered[t], 16)

            def split(t):
                x = e[:, t, :].rearrange("p (i d) -> p d i", d=D)
                part = [parts[:, t * D:(t + 1) * D, k, :] for k in range(PARTS)]
                pool.wait_ge(gathered[t], 16 * F)
                nc.gpsimd.tensor_copy(part[0], x).then_inc(split_step, 1)
                pool.wait_ge(split_step, 4 * t + 1)
                nc.gpsimd.tensor_tensor(rest[:, :, :], x, part[0], ALU.subtract).then_inc(split_step, 1)
                pool.wait_ge(split_step, 4 * t + 2)
                nc.gpsimd.tensor_copy(part[1], rest[:, :, :]).then_inc(split_step, 1)
                pool.wait_ge(split_step, 4 * t + 3)
                nc.gpsimd.tensor_tensor(part[2], rest[:, :, :], part[1], ALU.subtract).then_inc(split_step, 1)
                pool.wait_ge(split_step, 4 * t + 4)

            pool.wait_ge(ids_in, 16)
            for t in range(BT):
                gather(t)
                split(t)

        @block.tensor
        def _(pe):
            def transpose(c, more):
                n = chunk(c, more)
                pe.wait_ge(split_step, c[0] * 4 + ((c[1] + more) // Q * 4 + 4))
                if not at(c, FIRST) or more != 1:
                    pe.wait_ge(xp_ready, n)
                for j in range(DC):
                    lhs = parts[:, bass.ds(n * DC + j, 1), :, :].rearrange("p a k i -> p (a k i)")
                    last = nc.tensor.matmul(xt_ps[0:XR, j * P:(j + 1) * P], lhs, ident[:, :],
                                            start=True, stop=True)
                last.then_inc(transposed, 1)

            def spread_x(c, item):
                if item == 0:
                    pe.wait_ge(xp_ready, chunk(c, 2))
                if item == RING:
                    pe.wait_ge(x3_ready, chunk(c, 2))
                m = XR if item == 0 else (K0 + K1)[item - 1]
                slot = (c[1] + 1 if item <= T0 else c[1]) % Q
                nc.tensor.matmul(ring[item % RING][0:m, :], spread[:, item, 0:m], xp[:, slot, :],
                                 start=True, stop=True).then_inc(x3_spread if item == 0 else spread_done, 1)

            def contract(c, k):
                if k == 0 and not at(c, FIRST):
                    pe.wait_ge(h_ready, chunk(c, 1))
                if k == T0 and not at(c, (0, 0)):
                    pe.wait_ge(cur1_ready, chunk(c))
                pe.wait_ge(prod_ready, made(c, k + 1))
                z = prod[:, (k + 1) % RING, :]
                if k < T0:
                    ins = nc.tensor.matmul(acc0[:, :], w0_sum[0:K0[k], k, :], z[0:K0[k], :],
                                           start=(k == 0), stop=(k == T0 - 1))
                else:
                    t = k - T0
                    ins = nc.tensor.matmul(acc1[:, :], w1_sb[0:K1[t], t, :], z[0:K1[t], :],
                                           start=(t == 0), stop=(t == T1 - 1))
                ins.then_inc(contracted, 1)

            def step(c, following):
                now = [(c, m) for m in items(c)]
                stream = now + ([(following, m) for m in items(following)[:AHEAD]] if following else [])
                for at, (_, item) in enumerate(now):
                    if at + AHEAD < len(stream):
                        spread_x(*stream[at + AHEAD])
                    if item > 0:
                        contract(c, item - 1)
                    if item == T_AT and known_after(c, 2):
                        transpose(c, 2)

            pe.wait_ge(ident_in, 16)
            transpose(FIRST, 1)
            pe.wait_ge(spread_in, 16)
            for m in items(FIRST)[:AHEAD]:
                spread_x(FIRST, m)
            transpose(FIRST, 2)
            pe.wait_ge(w0_ready, 1)
            pe.wait_ge(w1_in, 32)
            step(FIRST, (0, 0))
            run_steps(pe, step)

            pe.wait_ge(mlp_in, MLP_IN)
            pe.wait_ge(zin_step, 2)
            for m in range(M1):
                cols = slice(m * P, (m + 1) * P)
                nc.tensor.matmul(ring[m][:, :], wt1_a[:, cols], zin_a[:, :], start=True, stop=False)
                nc.tensor.matmul(ring[m][:, :], wt1_b[:, cols], zin_b[:, :],
                                 start=False, stop=True).then_inc(h1_mm, 1)
            for k in range(M1):
                pe.wait_ge(h1_ready, k + 1)
                for m in range(M2):
                    last = nc.tensor.matmul((acc0, acc1)[m][:, :], wt2_sb[:, k, m * P:(m + 1) * P],
                                            h1_sb[:, k, :], start=(k == 0), stop=(k == M1 - 1))
                    if k == M1 - 1:
                        last.then_inc(h2_mm, 1)
            for m in range(M2):
                pe.wait_ge(h2_ready, m + 1)
                last = nc.tensor.matmul(y_ps[0:1, :], wt3_sb[:, m:m + 1], h2_sb[:, m, :],
                                        start=(m == 0), stop=(m == M2 - 1))
            last.then_inc(y_mm, 1)

        @block.scalar
        def _(act):
            def take_xp(c, more):
                act.wait_ge(transposed, chunk(c, more + 1))
                nc.scalar.activation(xp[:, (c[1] + more) % Q, :], xt_ps[0:XR, :],
                                     ACT.Copy).then_inc(xp_ready, 1)

            def take_x3(c, more):
                act.wait_ge(x3_spread, chunk(c, more + 1))
                nc.scalar.activation(x3[:, :], ring[0][0:XR, :], ACT.Copy).then_inc(x3_ready, 1)

            def take_h(c):
                act.wait_ge(contracted, made(c, T0))
                h = hh[:, (c[1] + 1) % 2, :]
                nc.scalar.activation(h[0:NF1, :], acc0[0:NF1, :], ACT.Relu)
                nc.scalar.activation(h[NF1:P, :], acc0[0:NF1, :], ACT.Relu)
                nc.scalar.activation(direct[NF1:P, :], acc0[NF1:P, :], ACT.Relu).then_inc(h_ready, 1)

            def step(c, following):
                if known_after(c, 1):
                    take_h(c)
                if known_after(c, 2):
                    take_xp(c, 2)
                    take_x3(c, 2)
                act.wait_ge(contracted, made(c, PER))
                nc.scalar.activation(cur1[:, :], acc1[:, :], ACT.Relu).then_inc(cur1_ready, 1)

            take_xp(FIRST, 1)
            take_x3(FIRST, 1)
            take_xp(FIRST, 2)
            take_h(FIRST)
            take_x3(FIRST, 2)
            run_steps(act, step)

            act.wait_ge(mlp_in, MLP_IN)
            for m in range(M1):
                act.wait_ge(h1_mm, m + 1)
                nc.scalar.activation(h1_sb[:, m, :], ring[m][:, :], ACT.Relu,
                                     bias=b1_sb[:, m:m + 1]).then_inc(h1_ready, 1)
            for m in range(M2):
                act.wait_ge(h2_mm, m + 1)
                nc.scalar.activation(h2_sb[:, m, :], (acc0, acc1)[m][:, :], ACT.Relu,
                                     bias=b2_sb[:, m:m + 1]).then_inc(h2_ready, 1)
            act.wait_ge(y_mm, 1)
            nc.scalar.activation(y_sb[:, :], y_ps[0:1, :], ACT.Copy).then_inc(y_ready, 1)

        @block.vector
        def _(dve):
            def product(c, k):
                if k == 0:
                    dve.wait_ge(x3_ready, chunk(c, 2))
                if k == T0:
                    dve.wait_ge(h_ready, chunk(c, 1))
                dve.wait_ge(spread_done, made(c, k + 1))
                since = RING - 1 if 0 < k + 1 < RING else RING
                if not (isinstance(c[0], int) and made(c, k) < since):
                    dve.wait_ge(contracted, made(c, k + 1 - since))
                item = k + 1
                m = (K0 + K1)[k]
                other = x3 if k < T0 else hh[:, c[1] % 2, :]
                nc.vector.tensor_tensor(prod[0:m, item % RING, :], ring[item % RING][0:m, :],
                                        other[0:m, :], ALU.mult).then_inc(prod_ready, 1)

            def sum_direct(c):
                dve.wait_ge(h_ready, chunk(c, 2))
                n = chunk(c, 1)
                nc.vector.tensor_reduce(direct_q[NF1:P, bass.ds(n, 1), :].rearrange("p a b -> p (a b)"),
                                        direct[NF1:P, :].rearrange("p (d b) -> p b d", d=DC),
                                        AX_X, ALU.add).then_inc(direct_summed, 1)

            def sum_cur1(c, more):
                dve.wait_ge(cur1_ready, chunk(c, more + 1))
                n = chunk(c, more)
                nc.vector.tensor_reduce(cur1_q[:, bass.ds(n, 1), :].rearrange("p a b -> p (a b)"),
                                        cur1[:, :].rearrange("p (d b) -> p b d", d=DC),
                                        AX_X, ALU.add).then_inc(cur1_summed, 1)

            def step(c, following):
                for k in products(c):
                    product(c, k)
                    if at(c, FIRST):
                        continue
                    if k == (CUR1_SUM_AT if not at(c, LAST) else T0) and not at(c, (0, 0)):
                        sum_cur1(c, -1)
                    if k == DIRECT_SUM_AT and not at(c, LAST):
                        sum_direct(c)

            nc.vector.memset(wt1_a[:, :], 0.0).then_inc(zeroed, 1)
            nc.vector.memset(zin_a[:, :], 0.0).then_inc(zeroed, 1)
            dve.wait_ge(w0_in, 32)
            nc.vector.tensor_tensor(w0_sum[:, :, :], w0_ij[:, :, :], w0_ji[:, :, :],
                                    ALU.add).then_inc(w0_ready, 1)
            step(FIRST, None)
            sum_direct(FIRST)
            run_steps(dve, step)
            sum_cur1(LAST, 0)
            dve.wait_ge(direct_summed, CH)
            dve.wait_ge(cur1_summed, CH)
            dve.wait_ge(mlp_in, MLP_IN)
            nc.vector.tensor_reduce(zin_a[NF1:P, :].rearrange("p (t b) -> p t b", t=BT),
                                    direct_q[NF1:P, :, :].rearrange("p (t q) b -> p t b q", t=BT),
                                    AX_X, ALU.add).then_inc(zin_step, 1)
            nc.vector.tensor_reduce(zin_b[:, :].rearrange("p (t b) -> p t b", t=BT),
                                    cur1_q[:, :, :].rearrange("p (t q) b -> p t b q", t=BT),
                                    AX_X, ALU.add).then_inc(zin_step, 1)


def layer0_rows():
    ij = np.full((XR, T0), -1)
    ji = np.full((XR, T0), -1)
    for g in range(T0):
        for p in range(K0[g]):
            i, s = p % F, 3 * g + p // F
            j = (i + s) % F
            ij[p, g] = i * F + j
            ji[p, g] = j * F + i if s else -1
    return ij, ji


def kernel(**inputs):
    import ml_dtypes
    import concourse.bacc as bacc
    from concourse.bass_utils import run_bass_kernel_spmd

    a = {k: np.ascontiguousarray(v) for k, v in inputs.items()}
    w0 = np.concatenate([a["L0_rec_W0"], np.zeros((1, L), np.float32)])
    ij, ji = layer0_rows()
    arrays = {
        "ids": np.ascontiguousarray(a["ids"].reshape(BT, P, F).transpose(1, 0, 2)).reshape(P, BT * F),
        "dense_t": np.ascontiguousarray(a["dense_ctx"].T),
        **{f"tbl_{f}": a[f"tbl_{f}"] for f in range(F)},
        "spread_c": spread_matrix().astype(ml_dtypes.bfloat16),
        "ident_c": np.eye(P, dtype=ml_dtypes.bfloat16),
        "w0a": w0[ij],
        "w0b": w0[ji],
        "w1": a["L0_rec_W1"],
        "wt1": a["W_top1"],
        "b1": np.ascontiguousarray(a["b_top1"].reshape(M1, P).T),
        "wt2": a["W_top2"],
        "b2": np.ascontiguousarray(a["b_top2"].reshape(M2, P).T),
        "wt3": np.ascontiguousarray(a["W_top3"].reshape(M2, P).T),
    }
    nc = bacc.Bacc("TRN2", target_bir_lowering=False, num_devices=1)
    t = {k: nc.dram_tensor(k, v.shape, mybir.dt.from_np(v.dtype), kind="ExternalInput").ap()
         for k, v in arrays.items()}
    out = nc.dram_tensor("y", (1, B), F32, kind="ExternalOutput").ap()
    tower(nc, t["ids"], t["dense_t"], [t[f"tbl_{f}"] for f in range(F)], t["spread_c"], t["ident_c"],
          t["w0a"], t["w0b"], t["w1"], t["wt1"], t["b1"], t["wt2"], t["b2"], t["wt3"], out)
    r = run_bass_kernel_spmd(nc, [arrays], core_ids=[0])
    return r.results[0]["y"].reshape(B, 1)
```

```python
from contextlib import ExitStack

import numpy as np
import concourse.bass as bass
from concourse import mybir

ALU = mybir.AluOpType
ACT = mybir.ActivationFunctionType
F32 = mybir.dt.float32
BF16 = mybir.dt.bfloat16
I32 = mybir.dt.int32
AX_X = mybir.AxisListType.X

P = 128
F = 39
D = 16
B = 512
NF1 = 64
L = 128
PARTS = 3
XR = PARTS * F
BT = B // P
DC = 4
NC = DC * P
Q = D // DC
CH = BT * Q
SHIFTS = F // 2 + 1
T0 = -(-SHIFTS // 3)
T1 = -(-F // 2)
K0 = [F * min(3, SHIFTS - 3 * g) for g in range(T0)]
K1 = [NF1 * min(2, F - 2 * t) for t in range(T1)]
RING = 4
GROUP = 4
AHEAD = RING - 1
PER = T0 + T1
ITEMS = 1 + PER
GROUPS = T1 // GROUP
H1, H2 = 512, 256
M1, M2 = H1 // P, H2 // P
DENSE = 16
T_AT = 10
CUR1_SUM_AT, DIRECT_SUM_AT = 3, T0 + 3
H1_AT, H2_AT, Y_AT, H1_DIRECT_AT = 12, 17, 22, 25
UNROLL = Q
LOOPS = (CH - 2) // UNROLL
PART_COLS = [(0, B - P), (B - P, B)]
FIRST_FIELDS = 32
assert ITEMS % RING == 0 and (1 + T0) % RING == 0 and T1 % GROUP == 0


def spread_matrix():
    cols = [[p % F for p in range(XR)]]
    cols += [[(p % F + 3 * g + p // F) % F for p in range(K0[g])] for g in range(T0)]
    m = np.zeros((XR, 1 + T0, P), np.float32)
    for c, picks in enumerate(cols):
        for p, i in enumerate(picks):
            m[i::F, c, p] = 1.0
    return m


def tower(nc, ids, dense_t, tables, spread_c, ident_c, w0a, w0b, w1, wt1, b1, wt2, b2, wt3, out):
    with ExitStack() as ctx:
        def sb(name, shape, dt=F32):
            return ctx.enter_context(nc.sbuf_tensor(name, shape, dt))

        def bank(name):
            return ctx.enter_context(nc.psum_tensor(name, [P, NC], F32))

        def sem(name):
            return ctx.enter_context(nc.semaphore(name))

        ids_sb = sb("ids_sb", [P, BT * F], I32)
        spread = sb("spread", [XR, 1 + T0, P], BF16)
        ident = sb("ident", [P, P], BF16)
        w0_ij = sb("w0_ij", [XR, T0, L])
        w0_ji = sb("w0_ji", [XR, T0, L])
        w0_sum = sb("w0_sum", [XR, T0, L])
        w1_sb = sb("w1_sb", [P, T1, L])
        wt1_a = sb("wt1_a", [P, H1])
        wt1_b = sb("wt1_b", [P, H1])
        wt2_sb = sb("wt2_sb", [P, M1, H2])
        wt3_sb = sb("wt3_sb", [P, M2])
        b1_sb = sb("b1_sb", [P, M1])
        b2_sb = sb("b2_sb", [P, M2])
        e = sb("e", [P, BT, F * D])
        rest = sb("rest", [P, D, F])
        x_rows = nc.dram_tensor("x_rows", [2, F + 1, NC], F32, kind="Internal").ap()
        parts = sb("parts", [P, BT * D, PARTS, F], BF16)
        xp = sb("xp", [XR, Q, NC], BF16)
        x3 = sb("x3", [XR, NC])
        opnd1 = sb("opnd1", [P, T1 + GROUP, NC])
        hh = sb("hh", [P, 2, NC])
        prod = sb("prod", [P, RING, NC])
        direct = sb("direct", [P, NC])
        cur1 = sb("cur1", [P, NC])
        direct_q = sb("direct_q", [P, CH, P])
        cur1_q = sb("cur1_q", [P, CH, P])
        zin_a = sb("zin_a", [P, B])
        zin_b = sb("zin_b", [P, B])
        cur1_pre = sb("cur1_pre", [P, P])
        h1_sb = sb("h1_sb", [P, M1, B])
        h2_sb = sb("h2_sb", [P, M2, B])
        y_sb = sb("y_sb", [1, B])

        ring = [bank(f"ring{r}") for r in range(RING)]
        acc0 = bank("acc0")
        acc1 = bank("acc1")
        xt_ps = bank("xt_ps")
        h2_ps = [xt_ps, bank("h2_ps")]

        ids_in = sem("ids_in")
        spread_in = sem("spread_in")
        ident_in = sem("ident_in")
        w0_in = sem("w0_in")
        w1_in = sem("w1_in")
        mlp_in = sem("mlp_in")
        gathered = [sem(f"gathered{t}") for t in range(BT)]
        gathered_first = sem("gathered_first")
        split_step = sem("split_step")
        split_first = sem("split_first")
        split_done = sem("split_done")
        x_stored = sem("x_stored")
        opnd1_in = [sem(f"opnd1_in{g}") for g in range(GROUPS + 1)]
        zeroed = sem("zeroed")
        w0_ready = sem("w0_ready")
        transposed = sem("transposed")
        xp_ready = sem("xp_ready")
        x3_spread = sem("x3_spread")
        x3_ready = sem("x3_ready")
        spread_done = sem("spread_done")
        prod_ready = sem("prod_ready")
        contracted = sem("contracted")
        h_ready = sem("h_ready")
        cur1_ready = sem("cur1_ready")
        direct_summed = sem("direct_summed")
        cur1_summed = sem("cur1_summed")
        cur1_pre_ready = sem("cur1_pre_ready")
        zin_a_ready = sem("zin_a_ready")
        zin_b_ready = sem("zin_b_ready")
        h1_mm = sem("h1_mm")
        h1_ready = sem("h1_ready")
        h2_mm = sem("h2_mm")
        h2_ready = sem("h2_ready")
        y_mm = sem("y_mm")
        y_ready = sem("y_ready")
        stored = sem("stored")

        block = ctx.enter_context(nc.Block())

        FIRST, LAST = (0, -1), (0, CH - 1)

        def chunk(c, more=0):
            return c[0] * UNROLL + (c[1] + more)

        def at(c, where):
            return isinstance(c[0], int) and c == where

        def made(c, k):
            if at(c, FIRST):
                return k
            return c[0] * (UNROLL * PER) + (T0 + c[1] * PER + k - (T0 if at(c, LAST) else 0))

        def spread_before(c, k):
            return k if at(c, FIRST) else c[0] * (UNROLL * T0) + (T0 + c[1] * T0 + k)

        def place1(parity, t):
            return T1 + t if t < GROUP and parity % 2 else t

        def products(c):
            return range(T0) if at(c, FIRST) else range(T0, PER) if at(c, LAST) else range(PER)

        def items(c):
            return ([] if at(c, LAST) else [0]) + [k + 1 for k in products(c)]

        def split(ops, engine, t, f0, f1, done, before):
            x = e[:, t, f0 * D:f1 * D].rearrange("p (i d) -> p d i", d=D)
            high, middle, low = (parts[:, t * D:(t + 1) * D, k, f0:f1] for k in range(PARTS))
            left = rest[:, :, f0:f1]
            ops.tensor_copy(high, x).then_inc(done, 1)
            engine.wait_ge(done, before + 1)
            ops.tensor_tensor(left, x, high, ALU.subtract).then_inc(done, 1)
            engine.wait_ge(done, before + 2)
            ops.tensor_copy(middle, left).then_inc(done, 1)
            engine.wait_ge(done, before + 3)
            return ops.tensor_tensor(low, left, middle, ALU.subtract)

        def run_steps(engine, step):
            step((0, 0), (0, 1))
            with engine.Fori(0, LOOPS) as i:
                for r in range(1, 1 + UNROLL):
                    step((i, r), (i, r + 1))
            for c in range(1 + LOOPS * UNROLL, CH):
                step((0, c), (0, c + 1) if c + 1 < CH else None)

        def known_after(c, n):
            return not isinstance(c[0], int) or c[1] + n < CH

        @block.sync
        def _(sp):
            sp.dma_start(ids_sb[:, :], ids).then_inc(ids_in, 16)
            sp.dma_start(ident[:, :], ident_c).then_inc(ident_in, 16)
            sp.dma_start(spread[:, :, :], spread_c).then_inc(spread_in, 16)
            def spread_by_dma(c):
                here = x_rows[(c[1] + 1) % 2]
                sp.wait_ge(x3_ready, chunk(c, 2))
                sp.dma_start(here[0:F, :], x3[0:F, :]).then_inc(x_stored, 16)
                sp.wait_ge(x_stored, 16 * chunk(c, 2))
                for g in range(GROUPS):
                    if g > 0 and not at(c, FIRST):
                        sp.wait_ge(prod_ready, made(c, T0 + GROUP * (g + 1)))
                    for half in range(2):
                        tiles = slice(g * GROUP, min((g + 1) * GROUP, (F - half + 1) // 2))
                        rows = here.rearrange("(t h) n -> h t n", h=2)[half, tiles, :]
                        places = [place1(c[1] + 1, t) for t in (tiles.start, tiles.stop - 1)]
                        sp.dma_start(opnd1[half * NF1:(half + 1) * NF1, places[0]:places[1] + 1, :],
                                     rows.partition_broadcast(NF1)
                                     ).then_inc(opnd1_in[places[0] // GROUP], 16)

            def step(c, following):
                if known_after(c, 1):
                    spread_by_dma(c)

            spread_by_dma(FIRST)
            run_steps(sp, step)
            sp.wait_ge(y_ready, len(PART_COLS))
            sp.dma_start(out, y_sb[:, :]).then_inc(stored, 16)
            sp.wait_ge(stored, 16)

        MLP_IN = 8 * 16

        @block.gpsimd
        def _(pool):
            def gather(t):
                for f in range(F):
                    pool.indirect_dma_start(
                        out=e[:, t, f * D:(f + 1) * D], out_offset=None, in_=tables[f],
                        in_offset=bass.IndirectOffsetOnAxis(
                            ap=ids_sb[:, t * F + f:t * F + f + 1], axis=0),
                    ).then_inc(gathered_first if t == 0 and f < FIRST_FIELDS else gathered[t], 16)

            pool.wait_ge(ids_in, 16)
            gather(0)
            for t in range(1, BT):
                gather(t)
                pool.wait_ge(gathered[t], 16 * F)
                pool.wait_ge(split_done, t)
                split(nc.gpsimd, pool, t, 0, F, split_step, 3 * (t - 1)).then_inc(split_done, 1)

        @block.tensor
        def _(pe):
            def transpose(c, more):
                n = chunk(c, more)
                pe.wait_ge(split_done, c[0] + ((c[1] + more) // Q + 1))
                if not at(c, FIRST) or more != 1:
                    pe.wait_ge(xp_ready, n)
                for j in range(DC):
                    lhs = parts[:, bass.ds(n * DC + j, 1), :, :].rearrange("p a k i -> p (a k i)")
                    last = nc.tensor.matmul(xt_ps[0:XR, j * P:(j + 1) * P], lhs, ident[:, :],
                                            start=True, stop=True)
                last.then_inc(transposed, 1)

            def spread_x(c, item):
                if item > T0:
                    return
                if item == 0:
                    pe.wait_ge(xp_ready, chunk(c, 2))
                if item == RING:
                    pe.wait_ge(x3_ready, chunk(c, 2))
                m = XR if item == 0 else K0[item - 1]
                nc.tensor.matmul(ring[item % RING][0:m, :], spread[:, item, 0:m],
                                 xp[:, (c[1] + 1) % Q, :],
                                 start=True, stop=True).then_inc(x3_spread if item == 0 else spread_done, 1)

            def contract(c, k):
                if k == 0 and not at(c, FIRST):
                    pe.wait_ge(h_ready, chunk(c, 1))
                if k == T0 and not at(c, (0, 0)):
                    pe.wait_ge(cur1_ready, chunk(c))
                pe.wait_ge(prod_ready, made(c, k + 1))
                z = prod[:, (k + 1) % RING, :]
                if k < T0:
                    ins = nc.tensor.matmul(acc0[:, :], w0_sum[0:K0[k], k, :], z[0:K0[k], :],
                                           start=(k == 0), stop=(k == T0 - 1))
                else:
                    t = k - T0
                    ins = nc.tensor.matmul(acc1[:, :], w1_sb[0:K1[t], t, :], z[0:K1[t], :],
                                           start=(t == 0), stop=(t == T1 - 1))
                ins.then_inc(contracted, 1)

            def mlp_h1(part, half):
                lo, hi = PART_COLS[part]
                pe.wait_ge(zin_b_ready if half else zin_a_ready, part + 1)
                for m in range(M1):
                    cols = slice(m * P, (m + 1) * P)
                    w, z = ((wt1_a, zin_a), (wt1_b, zin_b))[half]
                    ins = nc.tensor.matmul(ring[m][:, lo:hi], w[:, cols], z[:, lo:hi],
                                           start=(half == 0), stop=(half == 1))
                    if half:
                        ins.then_inc(h1_mm, 1)

            def mlp_h2(part):
                lo, hi = PART_COLS[part]
                for k in range(M1):
                    pe.wait_ge(h1_ready, part * M1 + k + 1)
                    for m in range(M2):
                        ins = nc.tensor.matmul(h2_ps[m][:, lo:hi], wt2_sb[:, k, m * P:(m + 1) * P],
                                               h1_sb[:, k, lo:hi], start=(k == 0), stop=(k == M1 - 1))
                        if k == M1 - 1:
                            ins.then_inc(h2_mm, 1)

            def mlp_y(part):
                lo, hi = PART_COLS[part]
                for m in range(M2):
                    pe.wait_ge(h2_ready, part * M2 + m + 1)
                    ins = nc.tensor.matmul(acc0[0:1, lo:hi], wt3_sb[:, m:m + 1], h2_sb[:, m, lo:hi],
                                           start=(m == 0), stop=(m == M2 - 1))
                ins.then_inc(y_mm, 1)

            def step(c, following):
                now = [(c, m) for m in items(c)]
                stream = now + ([(following, m) for m in items(following)[:AHEAD]] if following else [])
                for place, (_, item) in enumerate(now):
                    if place + AHEAD < len(stream):
                        spread_x(*stream[place + AHEAD])
                    if item > 0:
                        contract(c, item - 1)
                    if item == T_AT and known_after(c, 2):
                        transpose(c, 2)
                    if at(c, LAST):
                        if item == H1_AT:
                            pe.wait_ge(mlp_in, MLP_IN)
                            pe.wait_ge(h_ready, CH)
                            mlp_h1(0, 0)
                            mlp_h1(0, 1)
                        if item == H2_AT:
                            mlp_h2(0)
                        if item == Y_AT:
                            mlp_y(0)
                        if item == H1_DIRECT_AT:
                            pe.wait_ge(h1_ready, M1)
                            mlp_h1(1, 0)

            pe.wait_ge(ident_in, 16)
            transpose(FIRST, 1)
            pe.wait_ge(spread_in, 16)
            for m in items(FIRST)[:AHEAD]:
                spread_x(FIRST, m)
            transpose(FIRST, 2)
            pe.wait_ge(w0_ready, 1)
            pe.wait_ge(w1_in, 32)
            step(FIRST, (0, 0))
            run_steps(pe, step)

            mlp_h1(1, 1)
            mlp_h2(1)
            mlp_y(1)

        @block.scalar
        def _(act):
            act.dma_start(w0_ij[:, :, :], w0a).then_inc(w0_in, 16)
            act.dma_start(w0_ji[:, :, :], w0b).then_inc(w0_in, 16)
            whole = F * NF1 // P
            act.dma_start(w1_sb[:, 0:whole, :],
                         w1[0:whole * P, :].rearrange("(t p) l -> p t l", p=P)).then_inc(w1_in, 16)
            act.dma_start(w1_sb[0:K1[-1], whole, :], w1[whole * P:, :]).then_inc(w1_in, 16)
            act.wait_ge(zeroed, 2)
            act.dma_start(wt1_a[0:DENSE, :], wt1[NF1 + L:, :]).then_inc(mlp_in, 16)
            act.dma_start(wt1_a[NF1:P, :], wt1[0:NF1, :]).then_inc(mlp_in, 16)
            act.dma_start(wt1_b[:, :], wt1[NF1:NF1 + L, :]).then_inc(mlp_in, 16)
            act.dma_start(zin_a[0:DENSE, :], dense_t).then_inc(mlp_in, 16)
            act.dma_start(wt2_sb[:, :, :], wt2.rearrange("(m p) n -> p m n", p=P)).then_inc(mlp_in, 16)
            act.dma_start(wt3_sb[:, :], wt3).then_inc(mlp_in, 16)
            act.dma_start(b1_sb[:, :], b1).then_inc(mlp_in, 16)
            act.dma_start(b2_sb[:, :], b2).then_inc(mlp_in, 16)

            def take_xp(c, more):
                act.wait_ge(transposed, chunk(c, more + 1))
                nc.scalar.activation(xp[:, (c[1] + more) % Q, :], xt_ps[0:XR, :],
                                     ACT.Copy).then_inc(xp_ready, 1)

            def take_x3(c, more):
                if not (at(c, FIRST) and more == 1):
                    act.wait_ge(x_stored, 16 * chunk(c, more))
                act.wait_ge(x3_spread, chunk(c, more + 1))
                nc.scalar.activation(x3[:, :], ring[0][0:XR, :], ACT.Copy).then_inc(x3_ready, 1)

            def take_h(c):
                act.wait_ge(contracted, made(c, T0))
                h = hh[:, (c[1] + 1) % 2, :]
                nc.scalar.activation(h[0:NF1, :], acc0[0:NF1, :], ACT.Relu)
                nc.scalar.activation(h[NF1:P, :], acc0[0:NF1, :], ACT.Relu)
                nc.scalar.activation(direct[NF1:P, :], acc0[NF1:P, :], ACT.Relu).then_inc(h_ready, 1)

            def mlp(part):
                lo, hi = PART_COLS[part]
                act.wait_ge(mlp_in, MLP_IN)
                for m in range(M1):
                    act.wait_ge(h1_mm, part * M1 + m + 1)
                    nc.scalar.activation(h1_sb[:, m, lo:hi], ring[m][:, lo:hi], ACT.Relu,
                                         bias=b1_sb[:, m:m + 1]).then_inc(h1_ready, 1)
                for m in range(M2):
                    act.wait_ge(h2_mm, part * M2 + m + 1)
                    nc.scalar.activation(h2_sb[:, m, lo:hi], h2_ps[m][:, lo:hi], ACT.Relu,
                                         bias=b2_sb[:, m:m + 1]).then_inc(h2_ready, 1)
                act.wait_ge(y_mm, part + 1)
                nc.scalar.activation(y_sb[:, lo:hi], acc0[0:1, lo:hi], ACT.Copy).then_inc(y_ready, 1)

            def step(c, following):
                if at(c, LAST):
                    mlp(0)
                if known_after(c, 1):
                    take_h(c)
                if known_after(c, 2):
                    take_xp(c, 2)
                    take_x3(c, 2)
                act.wait_ge(contracted, made(c, PER))
                nc.scalar.activation(cur1[:, :], acc1[:, :], ACT.Relu).then_inc(cur1_ready, 1)

            take_xp(FIRST, 1)
            take_x3(FIRST, 1)
            take_xp(FIRST, 2)
            take_h(FIRST)
            take_x3(FIRST, 2)
            run_steps(act, step)

            mlp(1)

        @block.vector
        def _(dve):
            def product(c, k):
                if k == 0:
                    dve.wait_ge(x3_ready, chunk(c, 2))
                if k == T0:
                    dve.wait_ge(h_ready, chunk(c, 1))
                if k < T0:
                    dve.wait_ge(spread_done, spread_before(c, k + 1))
                elif (k - T0) % GROUP == 0:
                    group = place1(c[1], k - T0) // GROUP
                    if k == T0:
                        dve.wait_ge(opnd1_in[group], 32 * (c[0] * (UNROLL // 2) + (c[1] // 2 + 1)))
                    else:
                        dve.wait_ge(opnd1_in[group], 32 * chunk(c, 1))
                since = RING - 1 if 0 < k + 1 < RING else RING
                if not (isinstance(c[0], int) and made(c, k) < since):
                    dve.wait_ge(contracted, made(c, k + 1 - since))
                item = k + 1
                m = (K0 + K1)[k]
                x = ring[item % RING] if k < T0 else opnd1[:, place1(c[1], k - T0), :]
                other = x3 if k < T0 else hh[:, c[1] % 2, :]
                nc.vector.tensor_tensor(prod[0:m, item % RING, :], x[0:m, :],
                                        other[0:m, :], ALU.mult).then_inc(prod_ready, 1)

            def sum_direct(c):
                dve.wait_ge(h_ready, chunk(c, 2))
                n = chunk(c, 1)
                nc.vector.tensor_reduce(direct_q[NF1:P, bass.ds(n, 1), :].rearrange("p a b -> p (a b)"),
                                        direct[NF1:P, :].rearrange("p (d b) -> p b d", d=DC),
                                        AX_X, ALU.add).then_inc(direct_summed, 1)

            def sum_cur1(c, more):
                dve.wait_ge(cur1_ready, chunk(c, more + 1))
                n = chunk(c, more)
                nc.vector.tensor_reduce(cur1_q[:, bass.ds(n, 1), :].rearrange("p a b -> p (a b)"),
                                        cur1[:, :].rearrange("p (d b) -> p b d", d=DC),
                                        AX_X, ALU.add).then_inc(cur1_summed, 1)

            def zin(to, sums, p0, t0, t1, summed):
                dve.wait_ge(summed, Q * t1)
                dve.wait_ge(mlp_in, MLP_IN)
                return nc.vector.tensor_reduce(
                    to[p0:P, t0 * P:t1 * P].rearrange("p (t b) -> p t b", b=P),
                    sums[p0:P, t0 * Q:t1 * Q, :].rearrange("p (t q) b -> p t b q", q=Q),
                    AX_X, ALU.add)

            def step(c, following):
                for k in products(c):
                    product(c, k)
                    if at(c, FIRST):
                        continue
                    if k == (CUR1_SUM_AT if not at(c, LAST) else T0) and not at(c, (0, 0)):
                        sum_cur1(c, -1)
                    if k == DIRECT_SUM_AT and not at(c, LAST):
                        sum_direct(c)
                    if at(c, (0, CH - 3)) and k == PER - 1:
                        zin(zin_a, direct_q, NF1, 0, BT - 1, direct_summed).then_inc(zin_a_ready, 1)
                    if at(c, (0, CH - 2)) and k == PER - 1:
                        zin(zin_b, cur1_q, 0, 0, BT - 1, cur1_summed).then_inc(zin_b_ready, 1)
                    if at(c, LAST) and k == T0 + 2:
                        zin(zin_a, direct_q, NF1, BT - 1, BT, direct_summed).then_inc(zin_a_ready, 1)
                    if at(c, LAST) and k == T0 + 4:
                        dve.wait_ge(cur1_summed, CH - 1)
                        nc.vector.tensor_reduce(
                            cur1_pre[:, :], cur1_q[:, CH - Q:CH - 1, :].rearrange("p q b -> p b q"),
                            AX_X, ALU.add).then_inc(cur1_pre_ready, 1)

            nc.vector.memset(wt1_a[:, :], 0.0).then_inc(zeroed, 1)
            nc.vector.memset(zin_a[:, :], 0.0).then_inc(zeroed, 1)
            dve.wait_ge(w0_in, 32)
            nc.vector.tensor_tensor(w0_sum[:, :, :], w0_ij[:, :, :], w0_ji[:, :, :],
                                    ALU.add).then_inc(w0_ready, 1)
            dve.wait_ge(gathered_first, 16 * FIRST_FIELDS)
            split(nc.vector, dve, 0, 0, FIRST_FIELDS, split_first, 0)
            dve.wait_ge(gathered[0], 16 * (F - FIRST_FIELDS))
            split(nc.vector, dve, 0, FIRST_FIELDS, F, split_first, 3).then_inc(split_done, 1)
            step(FIRST, None)
            sum_direct(FIRST)
            run_steps(dve, step)
            sum_cur1(LAST, 0)
            dve.wait_ge(cur1_summed, CH)
            dve.wait_ge(cur1_pre_ready, 1)
            nc.vector.tensor_tensor(zin_b[:, B - P:B], cur1_pre[:, :], cur1_q[:, CH - 1, :],
                                    ALU.add).then_inc(zin_b_ready, 1)


def layer0_rows():
    ij = np.full((XR, T0), -1)
    ji = np.full((XR, T0), -1)
    for g in range(T0):
        for p in range(K0[g]):
            i, s = p % F, 3 * g + p // F
            j = (i + s) % F
            ij[p, g] = i * F + j
            ji[p, g] = j * F + i if s else -1
    return ij, ji


def kernel(**inputs):
    import ml_dtypes
    import concourse.bacc as bacc
    from concourse.bass_utils import run_bass_kernel_spmd

    a = {k: np.ascontiguousarray(v) for k, v in inputs.items()}
    w0 = np.concatenate([a["L0_rec_W0"], np.zeros((1, L), np.float32)])
    ij, ji = layer0_rows()
    arrays = {
        "ids": np.ascontiguousarray(a["ids"].reshape(BT, P, F).transpose(1, 0, 2)).reshape(P, BT * F),
        "dense_t": np.ascontiguousarray(a["dense_ctx"].T),
        **{f"tbl_{f}": a[f"tbl_{f}"] for f in range(F)},
        "spread_c": spread_matrix().astype(ml_dtypes.bfloat16),
        "ident_c": np.eye(P, dtype=ml_dtypes.bfloat16),
        "w0a": w0[ij],
        "w0b": w0[ji],
        "w1": a["L0_rec_W1"],
        "wt1": a["W_top1"],
        "b1": np.ascontiguousarray(a["b_top1"].reshape(M1, P).T),
        "wt2": a["W_top2"],
        "b2": np.ascontiguousarray(a["b_top2"].reshape(M2, P).T),
        "wt3": np.ascontiguousarray(a["W_top3"].reshape(M2, P).T),
    }
    nc = bacc.Bacc("TRN2", target_bir_lowering=False, num_devices=1)
    t = {k: nc.dram_tensor(k, v.shape, mybir.dt.from_np(v.dtype), kind="ExternalInput").ap()
         for k, v in arrays.items()}
    out = nc.dram_tensor("y", (1, B), F32, kind="ExternalOutput").ap()
    tower(nc, t["ids"], t["dense_t"], [t[f"tbl_{f}"] for f in range(F)], t["spread_c"], t["ident_c"],
          t["w0a"], t["w0b"], t["w1"], t["wt1"], t["b1"], t["wt2"], t["b2"], t["wt3"], out)
    r = run_bass_kernel_spmd(nc, [arrays], core_ids=[0])
    return r.results[0]["y"].reshape(B, 1)
```

```python
from contextlib import ExitStack

import numpy as np
import concourse.bass as bass
from concourse import mybir

ALU = mybir.AluOpType
ACT = mybir.ActivationFunctionType
F32 = mybir.dt.float32
I32 = mybir.dt.int32
AX_X = mybir.AxisListType.X

P = 128
R = 64
F = 39
D = 16
B = 512
NF1 = 64
L = 128
U = -(-F // 2)
FP = 2 * U
XR = 3 * FP
BT = B // R
DC = 8
NC = DC * R
Q = D // DC
CH = BT * Q
BLOCKS = [(k if k + P <= U * D else U * D - P, k) for k in range(0, U * D, P)]
UB = P // D
EARLY_GROUPS = [[0], []]
EARLY = len(EARLY_GROUPS)
SHIFTS = FP // 2 + 1
T0 = -(-SHIFTS // 3)
T1 = -(-F // 2)
K0 = [FP * sum(g + T0 * r < SHIFTS for r in range(3)) for g in range(T0)]
K1 = [NF1 * min(2, F - 2 * t) for t in range(T1)]
RING = 4
REPEATS = 2
UNROLL = 4
SLOTS = UNROLL // Q
GROUP = 4
PER = T0 + T1
GROUPS = T1 // GROUP
H1, H2 = 512, 256
M1, M2 = H1 // P, H2 // P
DENSE = 16
T_AT = 7
LATER = 6
STORE_AT = 0
CUR1_SUM_AT, DIRECT_SUM_AT, FIRST_SUM_AT = 3, T0 + 3, 3
H1_AT, H2_AT, Y_AT, H1_DIRECT_AT = 12, 16, 21, 24
LOOPS = (CH - 2) // UNROLL
LOTS0 = [(0, 2), (2, T0)]
PART_COLS = [(0, B - R), (B - R, B)]
assert T1 % GROUP == 0 and SHIFTS > 2 * T0 and UNROLL == 2 * Q


def turned(p):
    return (p % FP - T0 * (p // FP)) % FP


def tower(nc, ids, table_starts, dense_t, table, ident_c, w0a, w0b, w1, wt1, b1, wt2, b2, wt3, out):
    with ExitStack() as ctx:
        def sb(name, shape, dt=F32):
            return ctx.enter_context(nc.sbuf_tensor(name, shape, dt))

        def bank(name):
            return ctx.enter_context(nc.psum_tensor(name, [P, NC], F32))

        def sem(name):
            return ctx.enter_context(nc.semaphore(name))

        ids_sb = sb("ids_sb", [P, BT * U], I32)
        starts_sb = sb("starts_sb", [P, BT * U], I32)
        rows_sb = sb("rows_sb", [P, BT * U], I32)
        ident = sb("ident", [P, P])
        w0_ij = sb("w0_ij", [XR, T0, L])
        w0_ji = sb("w0_ji", [XR, T0, L])
        w0_sum = sb("w0_sum", [XR, T0, L])
        w1_sb = sb("w1_sb", [P, T1, L])
        wt1_a = sb("wt1_a", [P, H1])
        wt1_b = sb("wt1_b", [P, H1])
        wt2_sb = sb("wt2_sb", [P, M1, H2])
        wt3_sb = sb("wt3_sb", [P, M2])
        b1_sb = sb("b1_sb", [P, M1])
        b2_sb = sb("b2_sb", [P, M2])
        e = sb("e", [P, 2, U * D])
        x = sb("x", [P, len(BLOCKS), REPEATS, P])
        x_rows = nc.dram_tensor("x_rows", [SLOTS, REPEATS * FP, Q * NC], F32, kind="Internal").ap()
        x_turned = sb("x_turned", [XR, 2, NC])
        opnd0 = sb("opnd0", [XR, 2, T0, NC])
        opnd1 = sb("opnd1", [P, T1 + GROUP, NC])
        hh = sb("hh", [P, 2, NC])
        prod = sb("prod", [P, RING, NC])
        direct = sb("direct", [P, NC])
        cur1 = sb("cur1", [P, NC])
        direct_q = sb("direct_q", [P, CH, R])
        cur1_q = sb("cur1_q", [P, CH, R])
        zin_a = sb("zin_a", [P, B])
        zin_b = sb("zin_b", [P, B])
        h1_sb = sb("h1_sb", [P, M1, B])
        h2_sb = sb("h2_sb", [P, M2, B])
        y_sb = sb("y_sb", [1, B])

        acc0 = bank("acc0")
        acc1 = bank("acc1")
        spare = [bank(f"spare{n}") for n in range(6)]
        xt_ps = spare[:len(BLOCKS)]
        first_acc0 = spare[-1]
        h1_ps, h2_ps = spare[:M1], spare[M1:]

        ids_in = sem("ids_in")
        ident_in = sem("ident_in")
        w0_in = sem("w0_in")
        w1_in = sem("w1_in")
        mlp_in = sem("mlp_in")
        gathered = [[sem(f"gathered{s}_{j}") for j in range(len(BLOCKS))] for s in range(2)]
        rows_ready = sem("rows_ready")
        x_stored = sem("x_stored")
        early_stored = [sem(f"early_stored{j}") for j in range(EARLY)]
        turned_in = [sem(f"turned_in{s}") for s in range(2)]
        opnd0_in = [[sem(f"opnd0_in{s}_{n}") for n in range(len(LOTS0))] for s in range(2)]
        opnd1_in = [sem(f"opnd1_in{g}") for g in range(GROUPS + 1)]
        zeroed = sem("zeroed")
        w0_ready = sem("w0_ready")
        transposed = sem("transposed")
        x_ready = sem("x_ready")
        prod_ready = sem("prod_ready")
        contracted = sem("contracted")
        h_ready = sem("h_ready")
        cur1_ready = sem("cur1_ready")
        direct_summed = sem("direct_summed")
        cur1_summed = sem("cur1_summed")
        zin_a_ready = sem("zin_a_ready")
        zin_b_ready = sem("zin_b_ready")
        h1_mm = sem("h1_mm")
        h1_ready = sem("h1_ready")
        h2_mm = sem("h2_mm")
        h2_ready = sem("h2_ready")
        y_mm = sem("y_mm")
        y_ready = sem("y_ready")
        stored = sem("stored")

        block = ctx.enter_context(nc.Block())

        FIRST, LAST = (0, -1), (0, CH - 1)

        def chunk(c, more=0):
            return c[0] * UNROLL + (c[1] + more)

        def at(c, where):
            return isinstance(c[0], int) and c == where

        def made(c, k):
            if at(c, FIRST):
                return k
            return c[0] * (UNROLL * PER) + (T0 + c[1] * PER + k - (T0 if at(c, LAST) else 0))

        def place1(parity, t):
            return T1 + t if t < GROUP and parity % 2 else t

        def products(c):
            return range(T0) if at(c, FIRST) else range(T0, PER) if at(c, LAST) else range(PER)

        def of_parity(c, more):
            return c[0] * (UNROLL // 2) + ((c[1] + more) // 2 + 1)

        def tile(c, more):
            return c[0] * (UNROLL // Q) + (c[1] + more) // Q

        def tile_slot(c, more):
            return (c[1] + more) // Q % 2

        def chunk_rows(c, more):
            q = (c[1] + more) % Q
            return x_rows[tile_slot(c, more)][:, q * NC:(q + 1) * NC]

        def first_tile(t):
            return isinstance(t, int) and t == 0

        STORED = 16 * len(BLOCKS)

        def run_steps(engine, step):
            step((0, 0))
            with engine.Fori(0, LOOPS) as i:
                for r in range(1, 1 + UNROLL):
                    step((i, r))
            for c in range(1 + LOOPS * UNROLL, CH):
                step((0, c))

        def known_after(c, n):
            return not isinstance(c[0], int) or c[1] + n < CH

        @block.sync
        def _(sp):
            sp.dma_start(ids_sb[:, :], ids).then_inc(ids_in, 16)
            sp.dma_start(ident[:, :], ident_c).then_inc(ident_in, 16)

            def store(t, slot, j, stored):
                p = BLOCKS[j][1] - BLOCKS[j][0]
                sp.wait_ge(x_ready, t * len(BLOCKS) + (j + 1))
                to = bass.AP(x_rows.tensor, x_rows[slot].offset + BLOCKS[j][1] * R,
                             [[R, P - p], [U * Q * NC, 2 * REPEATS], [1, R]])
                sp.dma_start(to, x[p:P, j, :, :].rearrange("p k (o b) -> p (k o) b", b=R)
                             ).then_inc(stored, 16)

            def load0(c, more):
                sp.wait_ge(x_stored, tile(c, more) * STORED + (STORED - 16 * EARLY))
                rows, slot = chunk_rows(c, more), (c[1] + more) % 2
                for r in range(3):
                    first = -T0 * r % FP
                    sp.dma_start(x_turned[r * FP:(r + 1) * FP, slot, :],
                                 rows[first:first + FP, :]).then_inc(turned_in[slot], 16)
                for n, (g0, g1) in enumerate(LOTS0):
                    for r in range(3):
                        shifted = bass.AP(rows.tensor, rows.offset + g0 * Q * NC,
                                          [[Q * NC, FP], [Q * NC, g1 - g0], [1, NC]])
                        sp.dma_start(opnd0[r * FP:(r + 1) * FP, slot, g0:g1, :], shifted
                                     ).then_inc(opnd0_in[slot][n], 16)

            def load1(c, g):
                rows = chunk_rows(c, 1)[0:FP, :].rearrange("(t h) n -> h t n", h=2)
                for half in range(2):
                    last = min((g + 1) * GROUP, (F - half + 1) // 2) - 1
                    first, end = place1(c[1] + 1, g * GROUP), place1(c[1] + 1, last) + 1
                    sp.dma_start(opnd1[half * NF1:(half + 1) * NF1, first:end, :],
                                 rows[half, g * GROUP:last + 1, :].partition_broadcast(NF1)
                                 ).then_inc(opnd1_in[first // GROUP], 16)

            def step(c):
                for g in range(GROUPS):
                    if g == STORE_AT and known_after(c, 2):
                        if c[1] % 2 == 0:
                            for j in range(len(BLOCKS)):
                                store(tile(c, 2), tile_slot(c, 2), j, x_stored)
                        load0(c, 2)
                    if known_after(c, 1):
                        if g > 0:
                            sp.wait_ge(prod_ready, made(c, T0 + GROUP * (g + 1)))
                        load1(c, g)

            for j in range(EARLY):
                store(0, 0, j, early_stored[j])
                sp.wait_ge(early_stored[j], 16)
                for g in EARLY_GROUPS[j]:
                    load1(FIRST, g)
            store(0, 0, EARLY, x_stored)
            load0(FIRST, 1)
            load0(FIRST, 2)
            for g in range(GROUPS):
                if g not in sum(EARLY_GROUPS, []):
                    load1(FIRST, g)
            run_steps(sp, step)
            sp.wait_ge(y_ready, len(PART_COLS))
            sp.dma_start(out, y_sb[:, :]).then_inc(stored, 16)
            sp.wait_ge(stored, 16)

        MLP_IN = 8 * 16

        @block.gpsimd
        def _(pool):
            def gather(t):
                if t >= 2:
                    pool.wait_ge(transposed, len(BLOCKS) * (t - 1))
                for u in range(U):
                    n = R if u + U == F else P
                    at_u = t * U + u
                    pool.indirect_dma_start(
                        out=e[0:n, t % 2, u * D:(u + 1) * D], out_offset=None, in_=table,
                        in_offset=bass.IndirectOffsetOnAxis(ap=rows_sb[0:n, at_u:at_u + 1], axis=0),
                    ).then_inc(gathered[t % 2][u // UB], 16)

            pool.wait_ge(ids_in, 32)
            for n, cols in enumerate((slice(0, U), slice(U, BT * U))):
                nc.gpsimd.tensor_tensor(rows_sb[:, cols], ids_sb[:, cols], starts_sb[:, cols],
                                        ALU.add).then_inc(rows_ready, 1)
                pool.wait_ge(rows_ready, n + 1)
                if n == 0:
                    gather(0)
            for t in range(1, BT):
                gather(t)

        @block.tensor
        def _(pe):
            def transpose(t, slot, turns):
                for j, (k0, _) in enumerate(BLOCKS):
                    pe.wait_ge(gathered[slot][j], 16 * min(UB, U - j * UB) * turns)
                    if j == 0 and not first_tile(t):
                        pe.wait_ge(x_ready, t * len(BLOCKS))
                    nc.tensor.transpose(xt_ps[j][:, 0:P], e[:, slot, k0:k0 + P], ident[:, :]
                                        ).then_inc(transposed, 1)

            def contract(c, k):
                if k == 0 and not at(c, FIRST) and not at(c, (0, 0)):
                    pe.wait_ge(h_ready, chunk(c, 1))
                if k == T0 and not at(c, (0, 0)):
                    pe.wait_ge(cur1_ready, chunk(c))
                pe.wait_ge(prod_ready, made(c, k + 1))
                z = prod[:, (k + 1) % RING, :]
                if k < T0:
                    acc = first_acc0 if at(c, FIRST) else acc0
                    ins = nc.tensor.matmul(acc[:, :], w0_sum[0:K0[k], k, :], z[0:K0[k], :],
                                           start=(k == 0), stop=(k == T0 - 1))
                else:
                    t = k - T0
                    ins = nc.tensor.matmul(acc1[:, :], w1_sb[0:K1[t], t, :], z[0:K1[t], :],
                                           start=(t == 0), stop=(t == T1 - 1))
                ins.then_inc(contracted, 1)

            def mlp_h1(part, half):
                lo, hi = PART_COLS[part]
                pe.wait_ge(zin_b_ready if half else zin_a_ready, part + 1)
                for m in range(M1):
                    cols = slice(m * P, (m + 1) * P)
                    w, z = ((wt1_a, zin_a), (wt1_b, zin_b))[half]
                    ins = nc.tensor.matmul(h1_ps[m][:, lo:hi], w[:, cols], z[:, lo:hi],
                                           start=(half == 0), stop=(half == 1))
                    if half:
                        ins.then_inc(h1_mm, 1)

            def mlp_h2(part):
                lo, hi = PART_COLS[part]
                for k in range(M1):
                    pe.wait_ge(h1_ready, part * M1 + k + 1)
                    for m in range(M2):
                        ins = nc.tensor.matmul(h2_ps[m][:, lo:hi], wt2_sb[:, k, m * P:(m + 1) * P],
                                               h1_sb[:, k, lo:hi], start=(k == 0), stop=(k == M1 - 1))
                        if k == M1 - 1:
                            ins.then_inc(h2_mm, 1)

            def mlp_y(part):
                lo, hi = PART_COLS[part]
                for m in range(M2):
                    pe.wait_ge(h2_ready, part * M2 + m + 1)
                    ins = nc.tensor.matmul(acc0[0:1, lo:hi], wt3_sb[:, m:m + 1], h2_sb[:, m, lo:hi],
                                           start=(m == 0), stop=(m == M2 - 1))
                ins.then_inc(y_mm, 1)

            def step(c):
                for k in products(c):
                    contract(c, k)
                    if known_after(c, 2):
                        later = LATER if at(c, (0, 0)) else 0
                        if k == T_AT + later and c[1] % 2 == 0:
                            transpose(tile(c, 2), tile_slot(c, 2), c[0] + ((c[1] + 2) // UNROLL + 1))
                    if at(c, LAST):
                        if k == H1_AT:
                            pe.wait_ge(mlp_in, MLP_IN)
                            pe.wait_ge(h_ready, CH)
                            pe.wait_ge(x_ready, len(BLOCKS) * BT)
                            mlp_h1(0, 0)
                            mlp_h1(0, 1)
                        if k == H2_AT:
                            mlp_h2(0)
                        if k == Y_AT:
                            mlp_y(0)
                        if k == H1_DIRECT_AT:
                            pe.wait_ge(h1_ready, M1)
                            mlp_h1(1, 0)

            pe.wait_ge(ident_in, 16)
            pe.wait_ge(zeroed, 3)
            transpose(0, 0, 1)
            pe.wait_ge(w0_ready, 1)
            for k in products(FIRST):
                contract(FIRST, k)
            pe.wait_ge(w1_in, 32)
            run_steps(pe, step)

            mlp_h1(1, 1)
            mlp_h2(1)
            mlp_y(1)

        @block.scalar
        def _(act):
            act.dma_start(starts_sb[:, :], table_starts).then_inc(ids_in, 16)
            act.dma_start(w0_ij[:, :, :], w0a).then_inc(w0_in, 16)
            act.dma_start(w0_ji[:, :, :], w0b).then_inc(w0_in, 16)
            whole = F * NF1 // P
            act.dma_start(w1_sb[:, 0:whole, :],
                         w1[0:whole * P, :].rearrange("(t p) l -> p t l", p=P)).then_inc(w1_in, 16)
            act.dma_start(w1_sb[0:K1[-1], whole, :], w1[whole * P:, :]).then_inc(w1_in, 16)
            act.wait_ge(zeroed, 3)
            act.dma_start(wt1_a[0:DENSE, :], wt1[NF1 + L:, :]).then_inc(mlp_in, 16)
            act.dma_start(wt1_a[NF1:P, :], wt1[0:NF1, :]).then_inc(mlp_in, 16)
            act.dma_start(wt1_b[:, :], wt1[NF1:NF1 + L, :]).then_inc(mlp_in, 16)
            act.dma_start(zin_a[0:DENSE, :], dense_t).then_inc(mlp_in, 16)
            act.dma_start(wt2_sb[:, :, :], wt2.rearrange("(m p) n -> p m n", p=P)).then_inc(mlp_in, 16)
            act.dma_start(wt3_sb[:, :], wt3).then_inc(mlp_in, 16)
            act.dma_start(b1_sb[:, :], b1).then_inc(mlp_in, 16)
            act.dma_start(b2_sb[:, :], b2).then_inc(mlp_in, 16)

            def take_x(t):
                for j, (first, kept) in enumerate(BLOCKS):
                    p = kept - first
                    if j == 0 and not first_tile(t):
                        act.wait_ge(x_stored, t * STORED + (-16 * EARLY))
                    act.wait_ge(transposed, t * len(BLOCKS) + (j + 1))
                    repeated = xt_ps[j][p:P, 0:P].unsqueeze(1).broadcast_to([P - p, REPEATS, P])
                    nc.scalar.activation(x[p:P, j, :, :], repeated, ACT.Copy).then_inc(x_ready, 1)

            def take_h(c):
                act.wait_ge(contracted, made(c, T0))
                acc, h = first_acc0 if at(c, FIRST) else acc0, hh[:, (c[1] + 1) % 2, :]
                nc.scalar.activation(h[0:NF1, :], acc[0:NF1, :], ACT.Relu)
                nc.scalar.activation(h[NF1:P, :], acc[0:NF1, :], ACT.Relu)
                nc.scalar.activation(direct[NF1:P, :], acc[NF1:P, :], ACT.Relu).then_inc(h_ready, 1)

            def mlp(part):
                lo, hi = PART_COLS[part]
                act.wait_ge(mlp_in, MLP_IN)
                for m in range(M1):
                    act.wait_ge(h1_mm, part * M1 + m + 1)
                    nc.scalar.activation(h1_sb[:, m, lo:hi], h1_ps[m][:, lo:hi], ACT.Relu,
                                         bias=b1_sb[:, m:m + 1]).then_inc(h1_ready, 1)
                for m in range(M2):
                    act.wait_ge(h2_mm, part * M2 + m + 1)
                    nc.scalar.activation(h2_sb[:, m, lo:hi], h2_ps[m][:, lo:hi], ACT.Relu,
                                         bias=b2_sb[:, m:m + 1]).then_inc(h2_ready, 1)
                act.wait_ge(y_mm, part + 1)
                nc.scalar.activation(y_sb[:, lo:hi], acc0[0:1, lo:hi], ACT.Copy).then_inc(y_ready, 1)

            def step(c):
                if at(c, LAST):
                    mlp(0)
                if known_after(c, 1):
                    take_h(c)
                if known_after(c, 2) and c[1] % 2 == 0:
                    take_x(tile(c, 2))
                act.wait_ge(contracted, made(c, PER))
                nc.scalar.activation(cur1[:, :], acc1[:, :], ACT.Relu).then_inc(cur1_ready, 1)

            take_x(0)
            take_h(FIRST)
            run_steps(act, step)

            mlp(1)

        @block.vector
        def _(dve):
            def product(c, k):
                slot = (c[1] + 1) % 2
                if k == 0:
                    dve.wait_ge(turned_in[slot], 48 * of_parity(c, 1))
                for n, (g0, _) in enumerate(LOTS0):
                    if k == g0:
                        dve.wait_ge(opnd0_in[slot][n], 48 * of_parity(c, 1))
                if k == T0:
                    dve.wait_ge(h_ready, chunk(c, 1))
                    dve.wait_ge(opnd1_in[place1(c[1], 0) // GROUP],
                                32 * of_parity(c, 0))
                elif k > T0 and (k - T0) % GROUP == 0:
                    dve.wait_ge(opnd1_in[(k - T0) // GROUP], 32 * chunk(c, 1))
                since = RING - 1 if k + 1 < RING else RING
                if not (at(c, FIRST) and k < since):
                    dve.wait_ge(contracted, made(c, k + 1 - since))
                m = (K0 + K1)[k]
                if k >= T0:
                    own, other = opnd1[:, place1(c[1], k - T0), :], hh[:, c[1] % 2, :]
                else:
                    own, other = opnd0[:, slot, k, :], x_turned[:, slot, :]
                nc.vector.tensor_tensor(prod[0:m, (k + 1) % RING, :], own[0:m, :], other[0:m, :],
                                        ALU.mult).then_inc(prod_ready, 1)

            def sum_direct(c):
                dve.wait_ge(h_ready, chunk(c, 2))
                n = chunk(c, 1)
                nc.vector.tensor_reduce(direct_q[NF1:P, bass.ds(n, 1), :].rearrange("p a b -> p (a b)"),
                                        direct[NF1:P, :].rearrange("p (d b) -> p b d", d=DC),
                                        AX_X, ALU.add).then_inc(direct_summed, 1)

            def sum_cur1(c, more):
                dve.wait_ge(cur1_ready, chunk(c, more + 1))
                n = chunk(c, more)
                nc.vector.tensor_reduce(cur1_q[:, bass.ds(n, 1), :].rearrange("p a b -> p (a b)"),
                                        cur1[:, :].rearrange("p (d b) -> p b d", d=DC),
                                        AX_X, ALU.add).then_inc(cur1_summed, 1)

            def zin(to, sums, p0, t0, t1, summed):
                dve.wait_ge(summed, Q * t1)
                dve.wait_ge(mlp_in, MLP_IN)
                return nc.vector.tensor_reduce(
                    to[p0:P, t0 * R:t1 * R].rearrange("p (t b) -> p t b", b=R),
                    sums[p0:P, t0 * Q:t1 * Q, :].rearrange("p (t q) b -> p t b q", q=Q),
                    AX_X, ALU.add)

            def step(c):
                for k in products(c):
                    product(c, k)
                    if at(c, FIRST):
                        continue
                    if at(c, (0, 0)) and k == FIRST_SUM_AT:
                        sum_direct(FIRST)
                    if k == (CUR1_SUM_AT if not at(c, LAST) else T0) and not at(c, (0, 0)):
                        sum_cur1(c, -1)
                    if k == DIRECT_SUM_AT and not at(c, LAST):
                        sum_direct(c)
                    if at(c, (0, CH - 2)) and k == T0 + 8:
                        zin(zin_a, direct_q, NF1, 0, BT - 1, direct_summed).then_inc(zin_a_ready, 1)
                    if at(c, (0, CH - 2)) and k == PER - 1:
                        zin(zin_b, cur1_q, 0, 0, BT - 1, cur1_summed).then_inc(zin_b_ready, 1)
                    if at(c, LAST) and k == T0 + 2:
                        zin(zin_a, direct_q, NF1, BT - 1, BT, direct_summed).then_inc(zin_a_ready, 1)

            nc.vector.memset(wt1_a[:, :], 0.0).then_inc(zeroed, 1)
            nc.vector.memset(zin_a[:, :], 0.0).then_inc(zeroed, 1)
            nc.vector.memset(e[R:P, :, (U - 1) * D:U * D], 0.0).then_inc(zeroed, 1)
            dve.wait_ge(w0_in, 32)
            nc.vector.tensor_tensor(w0_sum[:, :, :], w0_ij[:, :, :], w0_ji[:, :, :],
                                    ALU.add).then_inc(w0_ready, 1)
            step(FIRST)
            run_steps(dve, step)
            sum_cur1(LAST, 0)
            zin(zin_b, cur1_q, 0, BT - 1, BT, cur1_summed).then_inc(zin_b_ready, 1)


def layer0_rows():
    ij = np.full((XR, T0), -1)
    ji = np.full((XR, T0), -1)
    taken = set()
    for g in range(T0):
        for p in range(K0[g]):
            i, j = turned(p), (p + g) % FP
            if max(i, j) < F and frozenset((i, j)) not in taken:
                taken.add(frozenset((i, j)))
                ij[p, g] = i * F + j
                ji[p, g] = j * F + i if i != j else -1
    return ij, ji


def by_gather(x):
    x = np.concatenate([x, np.zeros((B, 2 * U - F), x.dtype)], axis=1)
    return np.ascontiguousarray(x.reshape(BT, R, 2, U).transpose(2, 1, 0, 3)).reshape(P, BT * U)


def kernel(**inputs):
    import concourse.bacc as bacc
    from concourse.bass_utils import run_bass_kernel_spmd

    a = {k: np.ascontiguousarray(v) for k, v in inputs.items()}
    w0 = np.concatenate([a["L0_rec_W0"], np.zeros((1, L), np.float32)])
    ij, ji = layer0_rows()
    tables = [a[f"tbl_{f}"] for f in range(F)]
    starts = np.cumsum([0] + [len(t) for t in tables[:-1]]).astype(np.int32)
    arrays = {
        "ids": by_gather(a["ids"]),
        "table_starts": by_gather(np.broadcast_to(starts, (B, F))),
        "dense_t": np.ascontiguousarray(a["dense_ctx"].T),
        "table": np.concatenate(tables),
        "ident_c": np.eye(P, dtype=np.float32),
        "w0a": w0[ij],
        "w0b": w0[ji],
        "w1": a["L0_rec_W1"],
        "wt1": a["W_top1"],
        "b1": np.ascontiguousarray(a["b_top1"].reshape(M1, P).T),
        "wt2": a["W_top2"],
        "b2": np.ascontiguousarray(a["b_top2"].reshape(M2, P).T),
        "wt3": np.ascontiguousarray(a["W_top3"].reshape(M2, P).T),
    }
    nc = bacc.Bacc("TRN2", target_bir_lowering=False, num_devices=1)
    t = {k: nc.dram_tensor(k, v.shape, mybir.dt.from_np(v.dtype), kind="ExternalInput").ap()
         for k, v in arrays.items()}
    out = nc.dram_tensor("y", (1, B), F32, kind="ExternalOutput").ap()
    tower(nc, t["ids"], t["table_starts"], t["dense_t"], t["table"], t["ident_c"],
          t["w0a"], t["w0b"], t["w1"], t["wt1"], t["b1"], t["wt2"], t["b2"], t["wt3"], out)
    r = run_bass_kernel_spmd(nc, [arrays], core_ids=[0])
    return r.results[0]["y"].reshape(B, 1)
```
